# Optimizing a Trainium2 kernel written in Bass

```python
import numpy as np
import jax
import jax.numpy as jnp

def _softmax(x, axis=-1):
    return jax.nn.softmax(x, axis=axis)

def _gelu(x):
    return jax.nn.gelu(x, approximate=True)

def _silu(x):
    return jax.nn.silu(x)

def _sigmoid(x):
    return jax.nn.sigmoid(x)

def _layernorm(x, axis=-1, eps=1e-05):
    m = jnp.mean(x, axis=axis, keepdims=True)
    v = jnp.var(x, axis=axis, keepdims=True)
    return (x - m) / jnp.sqrt(v + eps)

def _scatter_add(tgt, idx, src, axis=0):
    return tgt.at[idx].add(src)

def _segment_sum(src, seg, n):
    return jax.ops.segment_sum(src, seg, n)
kernel_name = 'mk_lm_tower_d1_tok_ids1024_r4_0a50e3'

def setup_inputs(seed: int=0):
    np.random.seed(seed)
    _w = jnp.asarray

    def _rec_inputs():
        import jax
        import jax.numpy as jnp
        _rk = jax.random.key(seed)
        x = jax.random.randint(jax.random.fold_in(_rk, 1), (4, 512), 0, 31993, jnp.int32)
        return x
    x = _rec_inputs()

    def _L0_tok_setup():
        import jax, jax.numpy as jnp
        import numpy as np
        VOCAB = 8000
        DIM = 256
        key = jax.random.key(seed)
        k1, k2 = jax.random.split(key)
        token_ids = jax.random.randint(k1, (2, 1024), 0, VOCAB)
        e = jnp.clip(jax.random.normal(k2, (VOCAB, DIM), dtype=jnp.float32), -3.0, 3.0)
        return {'token_ids': token_ids, 'e': e}
    _L0_tok_all = _L0_tok_setup()
    _L0_tok_in = {k: v for k, v in _L0_tok_all.items() if k in ('e',)}
    del _L0_tok_all

    def _L0_attn_setup():
        import jax, jax.numpy as jnp
        import numpy as np
        DIM = 256
        HEADS = 16
        HEAD_DIM = DIM // HEADS

        def _xavier(key, shape):
            fan_out, fan_in = shape
            limit = float(np.sqrt(6.0 / (fan_in + fan_out)))
            return jax.random.uniform(key, shape, jnp.float32, -limit, limit)
        key = jax.random.key(seed)
        kx, kv, kk, kq = jax.random.split(key, 4)
        x = jax.random.normal(kx, (4, 512, DIM), jnp.float32)
        Wv = _xavier(kv, (DIM, DIM))
        Wk = _xavier(kk, (DIM, DIM))
        Wq = _xavier(kq, (DIM, DIM))
        return {'x': x, 'Wq': Wq, 'Wk': Wk, 'Wv': Wv}
    _L0_attn_all = _L0_attn_setup()
    _L0_attn_in = {k: v for k, v in _L0_attn_all.items() if k in ('Wq', 'Wk', 'Wv')}
    del _L0_attn_all

    def _L0_ffn_setup():
        import jax, jax.numpy as jnp
        import numpy as np
        DIM = 256

        def _reference_tuple_inner(x, W_r, W_k, W_v, mu_r, mu_k):
            B, T, C = x.shape
            x_prev = jnp.concatenate([jnp.zeros((B, 1, C), x.dtype), x[:, :-1, :]], axis=1)
            xr = mu_r * x + (1.0 - mu_r) * x_prev
            xk = mu_k * x + (1.0 - mu_k) * x_prev
            r = jax.nn.sigmoid(jnp.einsum('btc,dc->btd', xr, W_r))
            k = jnp.einsum('btc,dc->btd', xk, W_k)
            k_act = jnp.square(jax.nn.relu(k))
            out = r * jnp.einsum('btc,dc->btd', k_act, W_v)
            new_state = x[:, -1, :]
            return (out, new_state)
        key = jax.random.key(seed)
        ks = jax.random.split(key, 6)
        B, T, C = (8, 512, DIM)
        x = jax.random.normal(ks[0], (B, T, C), dtype=jnp.float32)
        s = 1.0 / np.sqrt(C)
        W_r = jax.random.uniform(ks[1], (C, C), jnp.float32, -s, s)
        W_k = jax.random.uniform(ks[2], (C, C), jnp.float32, -s, s)
        W_v = jax.random.uniform(ks[3], (C, C), jnp.float32, -s, s)
        mu_r = jax.random.uniform(ks[4], (C,), jnp.float32)
        mu_k = jax.random.uniform(ks[5], (C,), jnp.float32)
        return {'x': x, 'W_r': W_r, 'W_k': W_k, 'W_v': W_v, 'mu_r': mu_r, 'mu_k': mu_k}
    _L0_ffn_all = _L0_ffn_setup()
    _L0_ffn_in = {k: v for k, v in _L0_ffn_all.items() if k in ('W_r', 'W_k', 'W_v', 'mu_r', 'mu_k')}
    del _L0_ffn_all
    return {'x': x, 'L0_tok_e': _L0_tok_in['e'], 'L0_attn_Wq': _L0_attn_in['Wq'], 'L0_attn_Wk': _L0_attn_in['Wk'], 'L0_attn_Wv': _L0_attn_in['Wv'], 'L0_ffn_W_r': _L0_ffn_in['W_r'], 'L0_ffn_W_k': _L0_ffn_in['W_k'], 'L0_ffn_W_v': _L0_ffn_in['W_v'], 'L0_ffn_mu_r': _L0_ffn_in['mu_r'], 'L0_ffn_mu_k': _L0_ffn_in['mu_k']}

def reference(x, L0_tok_e, L0_attn_Wq, L0_attn_Wk, L0_attn_Wv, L0_ffn_W_r, L0_ffn_W_k, L0_ffn_W_v, L0_ffn_mu_r, L0_ffn_mu_k):
    import jax
    import jax.numpy as jnp

    def _L0_tok_ref(token_ids, e):
        import jax, jax.numpy as jnp
        import numpy as np
        VOCAB = 8000
        DIM = 256
        one_hot = jax.nn.one_hot(token_ids, VOCAB, dtype=e.dtype)
        return jnp.einsum('bsv,vd->bsd', one_hot, e)

    def _L0_attn_ref(x, Wq, Wk, Wv):
        import jax, jax.numpy as jnp
        import numpy as np
        DIM = 256
        HEADS = 16
        HEAD_DIM = DIM // HEADS

        def _xavier(key, shape):
            fan_out, fan_in = shape
            limit = float(np.sqrt(6.0 / (fan_in + fan_out)))
            return jax.random.uniform(key, shape, jnp.float32, -limit, limit)
        B, S, D = x.shape
        H, Hd = (HEADS, HEAD_DIM)
        q = (x @ Wq.T).reshape(B, S, H, Hd)
        k = (x @ Wk.T).reshape(B, S, H, Hd)
        v = (x @ Wv.T).reshape(B, S, H, Hd)
        energy = jnp.einsum('bqhd,bkhd->bhqk', q, k)
        attn = jax.nn.softmax(energy / jnp.sqrt(jnp.float32(D)), axis=-1)
        out = jnp.einsum('bhqk,bkhd->bqhd', attn, v).reshape(B, S, D)
        return out

    def _L0_ffn_ref(x, W_r, W_k, W_v, mu_r, mu_k):
        import jax, jax.numpy as jnp
        import numpy as np
        DIM = 256

        def _reference_tuple_inner(x, W_r, W_k, W_v, mu_r, mu_k):
            B, T, C = x.shape
            x_prev = jnp.concatenate([jnp.zeros((B, 1, C), x.dtype), x[:, :-1, :]], axis=1)
            xr = mu_r * x + (1.0 - mu_r) * x_prev
            xk = mu_k * x + (1.0 - mu_k) * x_prev
            r = jax.nn.sigmoid(jnp.einsum('btc,dc->btd', xr, W_r))
            k = jnp.einsum('btc,dc->btd', xk, W_k)
            k_act = jnp.square(jax.nn.relu(k))
            out = r * jnp.einsum('btc,dc->btd', k_act, W_v)
            new_state = x[:, -1, :]
            return (out, new_state)
        return _reference_tuple_inner(x, W_r, W_k, W_v, mu_r, mu_k)[0]
    h = _L0_tok_ref(x, L0_tok_e)
    h = h + _L0_attn_ref(_layernorm(h, axis=-1), L0_attn_Wq, L0_attn_Wk, L0_attn_Wv)
    h = h + _L0_ffn_ref(_layernorm(h, axis=-1), L0_ffn_W_r, L0_ffn_W_k, L0_ffn_W_v, L0_ffn_mu_r, L0_ffn_mu_k)
    return h

_drawn_inputs = setup_inputs


def setup_inputs(seed=0):
    import zlib

    import numpy as np

    out = dict(_drawn_inputs(seed))
    spreads = {}
    factors = {'L0_attn_Wq': 7.828, 'L0_attn_Wk': 7.806, 'L0_ffn_mu_r': 5.274}
    for name, (base, spread) in spreads.items():
        noise = np.random.default_rng([zlib.crc32(name.encode()), seed]).standard_normal(out[name].shape)
        drawn = base * np.exp(spread * noise) if base else spread * noise
        out[name] = jnp.asarray(drawn.astype(out[name].dtype))
    for name, factor in factors.items():
        out[name] = (out[name] * factor).astype(out[name].dtype)
    return out
```

```python
import concourse.bass as bass
from concourse import mybir
from contextlib import ExitStack

F32 = mybir.dt.float32
BF16 = mybir.dt.bfloat16
I32 = mybir.dt.int32
ALU = mybir.AluOpType
ACT = mybir.ActivationFunctionType
AX = mybir.AxisListType

B, T, C = 4, 512, 256
H, D = 16, 16
P = 128
NT = T // P
NC = C // P
GH = 4
NG = H // GH
VW = 32
LEAD = 6
SCALE = 1.0 / float(C) ** 0.5
EPS = 1e-5
Q_SLOTS = (0, 0, 0, 1, 1, 2)
K_SLOTS = (0, 1, 2, 0, 1, 0)
NS = len(Q_SLOTS)
KS = NS * D
NM = 3
WQ, WK, WV, WR, WF, WO = range(6)

TASKS = {
    (0, 1): ("oT", 2, -1), (2, 1): ("mT", 1, 0), (4, 0): ("xT", 0, 1), (4, 1): ("oT", 3, -1),
    (5, 0): ("xT", 1, 1), (5, 1): ("qk", 0, 1), (6, 0): ("qk", 1, 1), (6, 1): ("mT", 2, 0),
    (7, 0): ("qk", 2, 1), (7, 1): ("qk", 3, 1), (8, 0): ("yT", 0, -1), (8, 1): ("oT", 0, 0),
    (9, 0): ("v", 0, 1), (9, 1): ("yT", 1, -1), (10, 0): ("v", 1, 1), (10, 1): ("mT", 3, 0),
    (11, 0): ("fk", 0, -1), (11, 1): ("fk", 1, -1), (12, 0): ("fr", 0, -1), (12, 1): ("oT", 1, 0),
    (13, 0): ("fr", 1, -1), (13, 1): ("fv", 0, -1), (14, 0): ("fv", 1, -1), (14, 1): ("mT", 0, 1),
}
PER_BATCH = {"oT": NG, "mT": NG, "xT": NC, "qk": 2 * NC, "v": NT // 2, "yT": NC, "fk": NC, "fr": NT // 2,
             "fv": NT // 2}


def build(nc, ids, e, wq, wk, wv, wr, wf, wo, mu, out):
    ctx = ExitStack()
    with ctx:
        def sb(name, shape, dt=F32):
            return ctx.enter_context(nc.sbuf_tensor(name, shape, dt))

        def pb(name, shape, dt=F32):
            return ctx.enter_context(nc.psum_tensor(name, shape, dt))

        def sem(name):
            return ctx.enter_context(nc.semaphore(name))

        q_stack = sb("q_stack", [P, H, T], BF16)
        k_stack = sb("k_stack", [P, H, T], BF16)
        probs = sb("probs", [P, 2 * GH, NT, T])
        v_aug = sb("v_aug", [P, NT, H, VW])
        v_new = sb("v_new", [P, NT, H, D])
        h_all = sb("h_all", [P, B * NT, C])
        xn = sb("xn", [P, NT, C])
        xnT = sb("xnT", [P, NC, T])
        qk_part = sb("qk_part", [P, 2 * NC, 3, T], BF16)
        rest = sb("rest", [P, 2, T])
        pvT = sb("pvT", [P, T])
        attn = sb("attn", [P, NT, C])
        h2 = sb("h2", [P, NT, C])
        yn = sb("yn", [P, NT, C])
        ynT = sb("ynT", [P, NC, T + 1])
        dT = sb("dT", [P, NC, T])
        xrT = sb("xrT", [P, NC, T])
        xkT = sb("xkT", [P, NC, T])
        kaT = sb("kaT", [P, NC, T])
        tanh = sb("tanh", [P, NT, C])
        y = sb("y", [P, NT, C])
        wT = sb("wT", [P, 6, NC, C])
        w_nat = probs[:, 0:2, :, :].rearrange("p a b t -> p (a b t)")[:, 0:6 * NC * C].rearrange(
            "p (m r c) -> p m r c", m=6, r=NC)
        mu_c = sb("mu_c", [P, 2, NC])
        id_i = sb("id_i", [P, B * NT], I32)
        id_c = sb("id_c", [P, B * NT], I32)
        id_f = sb("id_f", [P, B * NT])
        id_g = sb("id_g", [P, B * NT])
        known = sb("known", [P, B * NT])
        ident = sb("ident", [P, P])
        ident_b = sb("ident_b", [P, P], BF16)
        stats = sb("stats", [P, NT, 6])
        mean_var = sb("mean_var", [P, 2, NT, 2])
        rstd = sb("rstd", [P, 2, NT])
        half = sb("half", [P, NT])
        neg_max = sb("neg_max", [P, 2, GH, NT])
        m_rest = sb("m_rest", [P, 2, GH * NT])
        m_part = sb("m_part", [P, NM, GH * NT], BF16)
        mT = sb("mT", [NM * GH * NT, P], BF16)
        rden = sb("rden", [P, NT, GH])
        ps_st = [pb(f"ps_st{i}", [P, 2, T]) for i in range(2)]
        ps_mx = [pb(f"ps_mx{i}", [P, T]) for i in range(2)]
        ps_pv = pb("ps_pv", [P, T])
        ps_bg = pb("ps_bg", [P, T])

        w_loaded, ids_loaded, mu_loaded = sem("w_loaded"), sem("ids_loaded"), sem("mu_loaded")
        gathered = [sem(f"gathered{i}") for i in range(B)]
        ids_ready, ident_zero, ident_ready = sem("ids_ready"), sem("ident_zero"), sem("ident_ready")
        id_step, consts_ready, masked = sem("id_step"), sem("consts_ready"), sem("masked")
        w_psum, w_ready = sem("w_psum"), sem("w_ready")
        st_ready, exp_done = sem("st_ready"), sem("exp_done")
        mx_ready, mx_reduced = sem("mx_ready"), sem("mx_reduced")
        pv_done, pvT_ready = sem("pv_done"), sem("pvT_ready")
        filled = [sem(f"filled{g}") for g in range(NG)]
        m_filled = [sem(f"m_filled{i}") for i in range(2)]
        m_step, m_split = sem("m_step"), sem("m_split")
        v_copied = sem("v_copied")
        part1_ready, rest_ready, part2_ready, rest2_ready, part3_ready = (
            sem("part1_ready"), sem("rest_ready"), sem("part2_ready"), sem("rest2_ready"), sem("part3_ready"))
        ln_stats = [sem("ln1_stats"), sem("ln2_stats")]
        ln_var = [sem("ln1_var"), sem("ln2_var")]
        ln_veps = [sem("ln1_veps"), sem("ln2_veps")]
        ln_rstd = [sem("ln1_rstd"), sem("ln2_rstd")]
        ln_done = [sem("ln1_done"), sem("ln2_done")]
        rden_ready, h2_ready = sem("rden_ready"), sem("h2_ready")
        d_ready, mixed, squared = sem("d_ready"), sem("mixed"), sem("squared")
        y_ready, out_done = sem("y_ready"), sem("out_done")
        start_done = sem("start_done")
        full = {k: sem(f"{k}_full") for k in PER_BATCH}
        taken = {k: sem(f"{k}_taken") for k in PER_BATCH}

        def wait(eng, s, value):
            if not isinstance(value, int) or value > 0:
                eng.wait_ge(s, value)

        def nth(kind, i, b):
            return PER_BATCH[kind] * b + (i + 1)

        def tasks_of(cur, nxt, prv):
            on = {0: cur, 1: nxt, -1: prv}
            return {at: t for at, t in TASKS.items() if on[t[2]]}

        block = ctx.enter_context(nc.Block())

        def evacuate_weight(copy, m):
            banks = [ps_st[0][:, 0, :], ps_st[0][:, 1, :], ps_st[1][:, 0, :], ps_st[1][:, 1, :], ps_mx[0][:], ps_mx[1][:]]
            for c in range(NC):
                src = banks[m][:, c * C:(c + 1) * C]
                dst = wT[:, m, c, :]
                if m in (WQ, WK):
                    src = src.rearrange("p (g h d) -> p g h d", g=NG, h=GH)
                    dst = dst.rearrange("p (g d h) -> p g h d", g=NG, h=GH)
                copy(dst, src).then_inc(w_ready, 1)

        @block.sync
        def _(sp):
            nc.sync.dma_start(id_i[:], ids).then_inc(ids_loaded, 16)
            for m, w in ((WQ, wq), (WK, wk), (WV, wv), (WR, wr), (WF, wf), (WO, wo)):
                nc.sync.dma_start(w_nat[:, m, :, :], w.rearrange("(r p) c -> p r c", p=P)).then_inc(w_loaded, 16)
            nc.sync.dma_start(mu_c[:], mu).then_inc(mu_loaded, 16)

            def fill(g, b):
                tile, lo = g // 2, (g % 2) * GH * D
                wait(sp, part3_ready, 2 * NC * b + 2 * tile + 2)
                wait(sp, st_ready, 2 * H * b + (8 * g + 8 - 2 * H))
                for s in range(NS):
                    for stack, slots, qk in ((q_stack, Q_SLOTS, 0), (k_stack, K_SLOTS, 1)):
                        nc.sync.dma_start(stack[s * D:(s + 1) * D, g * GH:(g + 1) * GH, :],
                                          qk_part[lo:lo + GH * D, 2 * tile + qk, slots[s], :]
                                          ).then_inc(filled[g], 16)

            def fill_max(g, b):
                wait(sp, taken["mT"], nth("mT", g, b))
                wait(sp, st_ready, 2 * H * b + (8 * g + 8 - 2 * H))
                nc.sync.dma_start(q_stack[KS:KS + NM, g * GH:(g + 1) * GH, :], mT[:, :]).then_inc(m_filled[g % 2], 16)

            def iteration(b, cur, nxt, prv):
                for j in range(H):
                    if j == 0 and cur:
                        fill(3, b)
                    if j == 3 and cur:
                        fill_max(1, b)
                    if j == 7:
                        if cur:
                            fill_max(2, b)
                        if nxt:
                            fill(0, b + 1)
                    if j == 8 and nxt:
                        fill(1, b + 1)
                    if j == 11 and cur:
                        fill_max(3, b)
                    if j == 12 and nxt:
                        fill(2, b + 1)
                    if j == 14 and prv:
                        for i in range(2):
                            wait(sp, y_ready, 2 * (b - 1) + i + 1)
                            rows = out[:, bass.ds((b - 1) * NT + 2 * i, 2), :]
                            nc.sync.dma_start(rows, y[:, 2 * i:2 * i + 2, :]).then_inc(out_done, 16)
                    if j == 15 and nxt:
                        fill_max(0, b + 1)

            iteration(-1, False, True, False)
            iteration(0, True, True, False)
            for b in range(1, B - 1):
                iteration(b, True, True, True)
            iteration(B - 1, True, False, True)
            iteration(B, False, False, True)
            sp.wait_ge(out_done, 2 * 16 * B)

        @block.gpsimd
        def _(pool):
            nc.gpsimd.memset(ident[:], 0.0).then_inc(ident_zero, 1)
            nc.gpsimd.memset(ident_b[:], 0.0).then_inc(ident_zero, 1)
            pool.wait_ge(ident_zero, 2)
            for m in (ident, ident_b):
                nc.gpsimd.affine_select(out=m[:], in_=m[:], compare_op=ALU.not_equal, fill=1.0, base=0,
                                        pattern=[[-1, P]], channel_multiplier=1).then_inc(ident_ready, 1)
            pool.wait_ge(ids_ready, 1)
            for t in range(B * NT):
                nc.gpsimd.indirect_dma_start(h_all[:, t, :], None, e, bass.IndirectOffsetOnAxis(ap=id_c[:, t:t + 1], axis=0)
                                             ).then_inc(gathered[t // NT], 16)
            nc.gpsimd.memset(half[:], -0.5).then_inc(start_done, 1)
            nc.gpsimd.memset(v_aug[:], 1.0).then_inc(consts_ready, 1)
            nc.gpsimd.memset(ynT[:, :, 0:1], 0.0).then_inc(consts_ready, 1)
            pool.wait_ge(start_done, 1)
            pool.wait_ge(consts_ready, 3)

            def rstd_of(ln, b):
                wait(pool, ln_stats[ln], b + 1)
                nc.gpsimd.tensor_scalar(rstd[:, ln, :], mean_var[:, ln, :, 1], EPS, None, ALU.add
                                        ).then_inc(ln_veps[ln], 1)
                wait(pool, ln_veps[ln], b + 1)
                nc.gpsimd.tensor_tensor(rstd[:, ln, :], rstd[:, ln, :], half[:], ALU.pow).then_inc(ln_rstd[ln], 1)

            def split_max(g, b):
                gi = NG * b + g
                wait(pool, mx_reduced, 16 * b + 16 * b * 3 + (16 * g + 16))
                nm = neg_max[:, g % 2, :, :].rearrange("p h t -> p (h t)")
                wait(pool, full["mT"], gi)
                nc.gpsimd.tensor_copy(m_part[:, 0, :], nm).then_inc(m_step, 1)
                wait(pool, m_step, 4 * gi + 1)
                nc.gpsimd.tensor_tensor(m_rest[:, 0, :], nm, m_part[:, 0, :], ALU.subtract).then_inc(m_step, 1)
                wait(pool, m_step, 4 * gi + 2)
                nc.gpsimd.tensor_copy(m_part[:, 1, :], m_rest[:, 0, :]).then_inc(m_step, 1)
                wait(pool, m_step, 4 * gi + 3)
                nc.gpsimd.tensor_tensor(m_rest[:, 1, :], m_rest[:, 0, :], m_part[:, 1, :], ALU.subtract).then_inc(m_step, 1)
                wait(pool, m_step, 4 * gi + 4)
                nc.gpsimd.tensor_copy(m_part[:, 2, :], m_rest[:, 1, :]).then_inc(m_split, 1)

            def split_qk(i, b):
                n = 2 * NC * b + i
                wait(pool, rest_ready, n + 1)
                for g in (2 * (i // 2), 2 * (i // 2) + 1):
                    wait(pool, filled[g], 16 * 2 * NS * b)
                nc.gpsimd.tensor_copy(qk_part[:, i, 1, :], rest[:, i % 2, :]).then_inc(part2_ready, 1)
                wait(pool, part2_ready, n + 1)
                nc.gpsimd.tensor_tensor(qk_part[:, i, 2, :], rest[:, i % 2, :], qk_part[:, i, 1, :], ALU.subtract
                                        ).then_inc(part3_ready, 1)

            def iteration(b, cur, nxt, prv):
                for j in range(H):
                    if j == 1 and nxt:
                        rstd_of(0, b + 1)
                    if j in (2, 6, 10) and cur:
                        split_max((j + 2) // 4, b)
                    if j == 14 and nxt:
                        split_max(0, b + 1)
                    if 1 <= j <= NT and cur:
                        kt = j - 1
                        wait(pool, taken["v"], nth("v", kt // 2, b))
                        wait(pool, pv_done, 4 * NG * b + (kt - 3))
                        nc.gpsimd.tensor_copy(v_aug[:, kt, :, 0:D], v_new[:, kt, :, :]).then_inc(v_copied, 1)
                    if j in (6, 7) and nxt:
                        for i in ((0, 1) if j == 6 else (2,)):
                            split_qk(i, b + 1)
                    if j == 8 and nxt:
                        split_qk(3, b + 1)
                    if j == 5 and prv:
                        wait(pool, taken["oT"], nth("oT", 3, b - 1))
                        wait(pool, y_ready, 2 * (b - 1))
                        nc.gpsimd.tensor_tensor(h2[:], h_all[:, bass.ds((b - 1) * NT, NT), :], attn[:], ALU.add
                                                ).then_inc(h2_ready, 1)
                    if j == 6 and prv:
                        rstd_of(1, b - 1)
                    if j in (9, 10) and prv:
                        c = j - 9
                        wait(pool, taken["yT"], nth("yT", c, b - 1))
                        wait(pool, mixed, 2 * NC * (b - 1))
                        nc.gpsimd.tensor_tensor(dT[:, c, :], ynT[:, c, 1:T + 1], ynT[:, c, 0:T], ALU.subtract
                                                ).then_inc(d_ready, 1)
                    if j == 11 and prv:
                        for c in range(NC):
                            wait(pool, taken["fk"], nth("fk", c, b - 1))
                            nc.gpsimd.tensor_tensor(kaT[:, c, :], kaT[:, c, :], kaT[:, c, :], ALU.mult
                                                    ).then_inc(squared, 1)

            iteration(-1, False, True, False)
            iteration(0, True, True, False)
            for b in range(1, B - 1):
                iteration(b, True, True, True)
            iteration(B - 1, True, False, True)
            iteration(B, False, False, True)

        @block.scalar
        def _(act):
            for m in (WQ, WV, WF):
                act.wait_ge(w_psum, m + 1)
                evacuate_weight(nc.scalar.copy, m)

            def exponentials(b, j, p):
                n = 2 * (H * b + j) + p
                wait(act, st_ready, n + 1)
                if p == 0 and j % GH == 0:
                    wait(act, pv_done, 4 * NG * b + (j - 4))
                nc.scalar.activation(probs[:, j % (2 * GH), 2 * p:2 * p + 2, :], ps_st[p][:, :, :], ACT.Exp,
                                     scale=SCALE).then_inc(exp_done, 1)

            def background(kind, i, b):
                if kind in ("oT", "fv"):
                    return
                wait(act, full[kind], nth(kind, i, b))
                if kind == "xT":
                    wait(act, full["v"], 2 * b)
                    nc.scalar.copy(xnT[:, i, :], ps_bg[:]).then_inc(taken[kind], 1)
                if kind == "qk":
                    for g in (2 * (i // 2), 2 * (i // 2) + 1):
                        wait(act, filled[g], 16 * 2 * NS * b)
                    nc.scalar.copy(qk_part[:, i, 0, :], ps_bg[:]).then_inc(part1_ready, 1)
                if kind == "v":
                    wait(act, v_copied, NT * b)
                    nc.scalar.copy(v_new[:, 2 * i:2 * i + 2, :, :].rearrange("p t h d -> p (t h d)"), ps_bg[:]
                                   ).then_inc(taken[kind], 1)
                if kind == "mT":
                    g = NG * b + i
                    wait(act, m_filled[(i + 1) % 2], 16 * (2 * b + (i + 1) // 2))
                    nc.scalar.copy(mT[:], ps_bg[0:NM * GH * NT, 0:P // 2].bitcast(BF16)).then_inc(taken[kind], 1)
                if kind == "yT":
                    wait(act, mixed, 2 * NC * b)
                    nc.scalar.copy(ynT[:, i, 1:T + 1], ps_bg[:]).then_inc(taken[kind], 1)
                if kind == "fk":
                    wait(act, full["fv"], 2 * b)
                    nc.scalar.activation(kaT[:, i, :], ps_bg[:], ACT.Relu).then_inc(taken[kind], 1)
                if kind == "fr":
                    wait(act, taken["fv"], 2 * b)
                    nc.scalar.activation(tanh[:, 2 * i:2 * i + 2, :].rearrange("p t c -> p (t c)"), ps_bg[:],
                                         ACT.Tanh, scale=0.5).then_inc(taken[kind], 1)

            def iteration(b, cur, nxt, prv):
                tasks = tasks_of(cur, nxt, prv)
                for j in range(H):
                    done = j // GH - 2 if j % GH == 0 else None
                    if done is not None and (cur if done >= 0 else prv):
                        wait(act, pv_done, 4 * NG * b + (4 * done + 4))
                        wait(act, full["oT"], NG * b + done)
                        nc.scalar.copy(pvT[:], ps_pv[:]).then_inc(pvT_ready, 1)
                    for p in range(2):
                        if cur:
                            exponentials(b, j, p)
                        if (j, p) in tasks:
                            kind, i, who = tasks[j, p]
                            background(kind, i, b + who)

            iteration(-1, False, True, False)
            iteration(0, True, True, False)
            for b in range(1, B - 1):
                iteration(b, True, True, True)
            iteration(B - 1, True, False, True)
            iteration(B, False, False, True)

        @block.vector
        def _(dve):
            vocab = e.shape[0]
            nc.vector.memset(k_stack[KS:KS + NM, :, :], 1.0).then_inc(consts_ready, 1)
            dve.wait_ge(ids_loaded, 16)
            nc.vector.tensor_copy(id_f[:], id_i[:]).then_inc(id_step, 1)
            dve.wait_ge(id_step, 1)
            nc.vector.tensor_scalar(id_g[:], id_f[:], 0.0, float(vocab - 1), ALU.max, ALU.min).then_inc(id_step, 1)
            dve.wait_ge(id_step, 2)
            nc.vector.tensor_copy(id_c[:], id_g[:]).then_inc(ids_ready, 1)
            nc.vector.tensor_tensor(known[:], id_f[:], id_g[:], ALU.is_equal).then_inc(id_step, 1)
            dve.wait_ge(id_step, 3)
            for m in (WK, WR, WO):
                dve.wait_ge(w_psum, m + 1)
                evacuate_weight(nc.vector.tensor_copy, m)
            for b in range(B):
                dve.wait_ge(gathered[b], 16 * NT)
                for t in range(b * NT, (b + 1) * NT):
                    nc.vector.tensor_scalar(h_all[:, t, :], h_all[:, t, :], known[:, t:t + 1], None, ALU.mult
                                            ).then_inc(masked, 1)
            dve.wait_ge(masked, B * NT)

            def ln_statistics(ln, b):
                for t in range(NT):
                    src = h_all[:, b * NT + t, :] if ln == 0 else h2[:, t, :]
                    nc.vector.bn_stats(stats[:, t, :], src).then_inc(ln_var[ln], 1)
                wait(dve, ln_var[ln], NT * (b + 1))
                for t in range(NT):
                    last = nc.vector.bn_aggr(mean_var[:, ln, t, :], stats[:, t, :])
                last.then_inc(ln_stats[ln], 1)

            def ln_apply(ln, b):
                wait(dve, ln_rstd[ln], b + 1)
                wait(dve, full["xT" if ln == 0 else "yT"], NC * b)
                for t in range(NT):
                    src = h_all[:, b * NT + t, :] if ln == 0 else h2[:, t, :]
                    last = nc.vector.tensor_scalar((xn, yn)[ln][:, t, :], src, mean_var[:, ln, t, 0:1],
                                                   rstd[:, ln, t:t + 1], ALU.subtract, ALU.mult)
                last.then_inc(ln_done[ln], 1)

            def maxima(b, head, g, tiles):
                for t in tiles:
                    n = 4 * H * b + (4 * head + t)
                    wait(dve, mx_ready, n + 1)
                    if head % GH == 0 and t == 0:
                        wait(dve, m_split, NG * b + (g - 1))
                    nc.vector.tensor_reduce(neg_max[:, g % 2, head % GH, t:t + 1], ps_mx[t % 2][:], AX.X, ALU.max,
                                            negate=True).then_inc(mx_reduced, 1)

            def background(kind, i, b):
                if kind == "qk":
                    n = 2 * NC * b + i
                    wait(dve, part1_ready, n + 1)
                    wait(dve, part3_ready, n - 1)
                    nc.vector.tensor_tensor(rest[:, i % 2, :], ps_bg[:], qk_part[:, i, 0, :], ALU.subtract
                                            ).then_inc(rest_ready, 1)
                if kind == "oT":
                    wait(dve, full["oT"], nth("oT", i, b))
                    sums = ps_bg[:, :].rearrange("p (t h w) -> p t h w", t=NT, h=GH)
                    nc.vector.reciprocal(rden[:], sums[:, :, :, D]).then_inc(rden_ready, 1)
                    wait(dve, rden_ready, NG * b + (i + 1))
                    if i == 0:
                        wait(dve, h2_ready, b)
                    dst = attn[:, :, i * GH * D:(i + 1) * GH * D].rearrange("p t (h d) -> p t h d", h=GH)
                    nc.vector.tensor_tensor(dst, sums[:, :, :, 0:D], rden[:, :, :].unsqueeze(3).broadcast_to([P, NT, GH, D]),
                                            ALU.mult).then_inc(taken["oT"], 1)
                if kind == "fv":
                    wait(dve, full["fv"], nth("fv", i, b))
                    wait(dve, taken["fr"], nth("fr", i, b))
                    wait(dve, out_done, 16 * 2 * b)
                    flat = lambda a: a[:, 2 * i:2 * i + 2, :].rearrange("p t c -> p (t c)")
                    nc.vector.scalar_tensor_tensor(flat(y), flat(tanh), 1.0, ps_bg[:], ALU.add, ALU.mult
                                                   ).then_inc(taken["fv"], 1)
                    wait(dve, taken["fv"], nth("fv", i, b))
                    nc.vector.scalar_tensor_tensor(flat(y), flat(y), 0.5, flat(h2), ALU.mult, ALU.add
                                                   ).then_inc(y_ready, 1)

            def iteration(b, cur, nxt, prv):
                tasks = tasks_of(cur, nxt, prv)
                for j in range(H):
                    if j == 0 and nxt:
                        ln_statistics(0, b + 1)
                    if j == 2 and nxt:
                        ln_apply(0, b + 1)
                    if j == 6 and prv:
                        wait(dve, h2_ready, b)
                        ln_statistics(1, b - 1)
                    if j == 7 and prv:
                        ln_apply(1, b - 1)
                    for p in range(2):
                        if (j, p) in tasks:
                            kind, i, who = tasks[j, p]
                            background(kind, i, b + who)
                        head = (j + LEAD) % H
                        ahead = (j + LEAD) // H
                        if nxt if ahead else cur:
                            maxima(b + ahead, head, head // GH, (2 * p, 2 * p + 1))
                    if j == 10 and prv:
                        if not cur:
                            pass
                        for c in range(NC):
                            wait(dve, d_ready, NC * (b - 1) + (c + 1))
                            wait(dve, full["fr"], 2 * (b - 1))
                            if c == 0:
                                wait(dve, mu_loaded, 16)
                            for m, dst in ((1, xkT), (0, xrT)):
                                nc.vector.scalar_tensor_tensor(dst[:, c, :], dT[:, c, :], mu_c[:, m, c:c + 1],
                                                               ynT[:, c, 0:T], ALU.mult, ALU.add).then_inc(mixed, 1)

            iteration(-1, False, True, False)
            iteration(0, True, True, False)
            for b in range(1, B - 1):
                iteration(b, True, True, True)
            iteration(B - 1, True, False, True)
            iteration(B, False, False, True)

        @block.tensor
        def _(pe):
            banks = [ps_st[0][:, 0, :], ps_st[0][:, 1, :], ps_st[1][:, 0, :], ps_st[1][:, 1, :], ps_mx[0][:], ps_mx[1][:]]
            pe.wait_ge(ident_ready, 2)
            pe.wait_ge(w_loaded, 6 * 16)
            for m in range(6):
                for c in range(NC):
                    for r in range(NC):
                        last = nc.tensor.transpose(banks[m][:, c * C + r * P:c * C + (r + 1) * P],
                                                   w_nat[:, m, r, c * P:(c + 1) * P], ident[:])
                last.then_inc(w_psum, 1)
            pe.wait_ge(w_ready, 6 * NC)
            pe.wait_ge(consts_ready, 3)

            def scores_transposed(b, j, p):
                n = 2 * (H * b + j) + p
                if p == 0 and j % GH == 0:
                    g = j // GH
                    wait(pe, m_filled[g % 2], 16 * (2 * b + (g // 2 + 1)))
                wait(pe, exp_done, n - 1)
                for i in range(2):
                    kt = 2 * p + i
                    last = nc.tensor.matmul(ps_st[p][:, i, :], k_stack[0:KS + NM, j, kt * P:(kt + 1) * P],
                                            q_stack[0:KS + NM, j, :], start=True, stop=True)
                last.then_inc(st_ready, 1)

            def scores_for_max(b, head, tiles):
                if head % GH == 0 and tiles[0] == 0:
                    wait(pe, filled[head // GH], 16 * 2 * NS * (b + 1))
                for t in tiles:
                    n = 4 * H * b + (4 * head + t)
                    wait(pe, mx_reduced, n - 1)
                    nc.tensor.matmul(ps_mx[t % 2][:], q_stack[0:KS, head, t * P:(t + 1) * P], k_stack[0:KS, head, :],
                                     start=True, stop=True).then_inc(mx_ready, 1)

            def weighted_sums(b, g, kt):
                gi = NG * b + g
                if kt == 0:
                    wait(pe, exp_done, 8 * gi + 8)
                    wait(pe, pvT_ready, gi)
                wait(pe, v_copied, NT * b + (kt + 1))
                for h in range(GH):
                    last = nc.tensor.matmul(ps_pv[h * VW:(h + 1) * VW, :], v_aug[:, kt, g * GH + h, :],
                                            probs[:, (g % 2) * GH + h, kt, :], start=(kt == 0), stop=(kt == NT - 1),
                                            tile_position=(0, h * VW))
                last.then_inc(pv_done, 1)

            def background(kind, i, b):
                mm, last = nc.tensor.matmul, None
                if kind in ("xT", "yT"):
                    ln = 0 if kind == "xT" else 1
                    wait(pe, ln_done[ln], b + 1)
                    for t in range(NT):
                        last = nc.tensor.transpose(ps_bg[:, t * P:(t + 1) * P], (xn, yn)[ln][:, t, i * P:(i + 1) * P],
                                                   ident[:])
                if kind == "qk":
                    wait(pe, taken["xT"], NC * (b + 1))
                    tile, m = i // 2, (WQ, WK)[i % 2]
                    for c in range(NC):
                        last = mm(ps_bg[:], wT[:, m, c, tile * P:(tile + 1) * P], xnT[:, c, :],
                                  start=(c == 0), stop=(c == NC - 1))
                if kind == "v":
                    for t in range(2):
                        for c in range(NC):
                            tok = 2 * i + t
                            last = mm(ps_bg[:, t * C:(t + 1) * C], xnT[:, c, tok * P:(tok + 1) * P], wT[:, WV, c, :],
                                      start=(c == 0), stop=(c == NC - 1))
                if kind == "mT":
                    wait(pe, m_split, NG * b + (i + 1))
                    last = nc.tensor.transpose(ps_bg[0:NM * GH * NT, 0:P // 2].bitcast(BF16),
                                               m_part[:, :, :].rearrange("p a n -> p (a n)"), ident_b[:])
                if kind == "oT":
                    wait(pe, pvT_ready, NG * b + (i + 1))
                    for t in range(NT):
                        last = nc.tensor.transpose(ps_bg[:, t * P:(t + 1) * P], pvT[:, t * P:(t + 1) * P], ident[:])
                if kind == "fk":
                    wait(pe, mixed, 2 * NC * (b + 1))
                    for c in range(NC):
                        last = mm(ps_bg[:], wT[:, WF, c, i * P:(i + 1) * P], xkT[:, c, :],
                                  start=(c == 0), stop=(c == NC - 1))
                if kind == "fr":
                    for t in range(2):
                        for c in range(NC):
                            tok = 2 * i + t
                            last = mm(ps_bg[:, t * C:(t + 1) * C], xrT[:, c, tok * P:(tok + 1) * P], wT[:, WR, c, :],
                                      start=(c == 0), stop=(c == NC - 1))
                if kind == "fv":
                    wait(pe, squared, NC * (b + 1))
                    for t in range(2):
                        for c in range(NC):
                            tok = 2 * i + t
                            last = mm(ps_bg[:, t * C:(t + 1) * C], kaT[:, c, tok * P:(tok + 1) * P], wT[:, WO, c, :],
                                      start=(c == 0), stop=(c == NC - 1))
                last.then_inc(full[kind], 1)

            def bank_free(task, b):
                kind, i, who = task
                s = rest_ready if kind == "qk" else taken[kind]
                wait(pe, s, nth(kind, i, b + who))

            def iteration(b, cur, nxt, prv, before=None):
                tasks = tasks_of(cur, nxt, prv)
                for j in range(H):
                    head, ahead = (j + LEAD) % H, (j + LEAD) // H
                    for p in range(2):
                        if cur:
                            scores_transposed(b, j, p)
                        if (j, p) in tasks:
                            kind, i, who = tasks[j, p]
                            if before:
                                bank_free(before[0], b + before[1])
                            background(kind, i, b + who)
                            before = (tasks[j, p], 0)
                        if nxt if ahead else cur:
                            scores_for_max(b + ahead, head, (2 * p, 2 * p + 1))
                    g = j // GH - 1
                    if cur if g >= 0 else prv:
                        weighted_sums(b + (0 if g >= 0 else -1), g % NG, j % GH)
                return before

            last_task = iteration(-1, False, True, False)
            last_task = iteration(0, True, True, False, (last_task[0], -1))
            for b in range(1, B - 1):
                last_task = iteration(b, True, True, True, (last_task[0], -1))
            last_task = iteration(B - 1, True, False, True, (last_task[0], -1))
            iteration(B, False, False, True, (last_task[0], -1))


def kernel(x, L0_tok_e, L0_attn_Wq, L0_attn_Wk, L0_attn_Wv, L0_ffn_W_r, L0_ffn_W_k, L0_ffn_W_v, L0_ffn_mu_r,
           L0_ffn_mu_k):
    import numpy as np
    import concourse.bacc as bacc
    from concourse.bass_utils import run_bass_kernel_spmd

    nc = bacc.Bacc("TRN2", target_bir_lowering=False, num_devices=1)
    arrays = {
        "ids": np.ascontiguousarray(np.asarray(x).reshape(B * NT, P).T),
        "e": np.asarray(L0_tok_e),
        "wq": np.asarray(L0_attn_Wq), "wk": np.asarray(L0_attn_Wk), "wv": np.asarray(L0_attn_Wv),
        "wr": np.asarray(L0_ffn_W_r), "wf": np.asarray(L0_ffn_W_k), "wo": np.asarray(L0_ffn_W_v),
        "mu": np.ascontiguousarray(np.stack([np.asarray(L0_ffn_mu_r), np.asarray(L0_ffn_mu_k)])
                                   .reshape(2, NC, P).transpose(2, 0, 1)),
    }
    args = [nc.dram_tensor(n, a.shape, mybir.dt.from_np(a.dtype), kind="ExternalInput").ap()
            for n, a in arrays.items()]
    out = nc.dram_tensor("out", (B * NT * P, C), F32, kind="ExternalOutput").ap()
    build(nc, *args, out.rearrange("(n p) c -> p n c", p=P))
    r = run_bass_kernel_spmd(nc, [arrays], core_ids=[0])
    return np.asarray(r.results[0]["out"]).reshape(B, T, C)
```

```python
import concourse.bass as bass
from concourse import mybir
from contextlib import ExitStack

F32 = mybir.dt.float32
BF16 = mybir.dt.bfloat16
I32 = mybir.dt.int32
ALU = mybir.AluOpType
ACT = mybir.ActivationFunctionType
AX = mybir.AxisListType

B, T, C = 4, 512, 256
H, D = 16, 16
P = 128
NT = T // P
NC = C // P
GH = 4
NG = H // GH
NH = H // NC
VW = 32
LEAD = 6
SCALE = 1.0 / float(C) ** 0.5
EPS = 1e-5
Q_SLOTS = (0, 0, 0, 1, 1, 2)
K_SLOTS = (0, 1, 2, 0, 1, 0)
NS = len(Q_SLOTS)
KS = NS * D
FILLS = sorted([(qk, part, s) for qk, slots in enumerate((Q_SLOTS, K_SLOTS)) for s, part in enumerate(slots)],
               key=lambda f: (f[0] + f[1], f[0]))
AT = {"mask": 9, "rstd1": 15, "gather": 1, "third01": 3, "third23": 10, "h2": 5, "rstd2": 9, "d": 12, "squares": 15, "fill0": 7, "out": 13}
POOL_FILLS = ((1, 1), (1, 4))
WARM = (36, 0, 0, 0)
NM = 3
WQ, WK, WV, WR, WF, WO = range(6)

TASKS = {
    (0, 0): ("fr", 0, -2), (0, 1): ("oT", 2, -1), (1, 0): ("fr", 1, -2), (1, 1): ("xT", 0, 1), (2, 0): ("xT", 1, 1),
    (2, 1): ("mT", 1, 0), (3, 0): ("qk", 0, 1), (4, 0): ("qk", 1, 1), (4, 1): ("oT", 3, -1), (5, 0): ("fv", 0, -2),
    (6, 0): ("qk", 2, 1), (6, 1): ("mT", 2, 0), (7, 0): ("qk", 3, 1), (7, 1): ("v", 0, 1), (8, 0): ("fv", 1, -2),
    (10, 0): ("oT", 0, 0), (10, 1): ("mT", 3, 0), (11, 0): ("v", 1, 1), (11, 1): ("yT", 0, -1),
    (12, 0): ("yT", 1, -1), (14, 0): ("fk", 0, -1), (14, 1): ("mT", 0, 1), (15, 0): ("fk", 1, -1),
    (15, 1): ("oT", 1, 0),
}
EXTRAS = {
    (0, 0): ("apply1", 0, 1), (0, 1): ("apply1", 1, 1), (0, 3): ("apply1", 2, 1), (1, 0): ("apply1", 3, 1),
    (5, 2): ("stats2", 0, -1), (6, 2): ("stats1", 0, 2), (7, 0): ("stats2", 1, -1), (7, 2): ("stats2", 2, -1),
    (7, 3): ("stats2", 3, -1), (9, 0): ("aggr2", 0, -1), (9, 1): ("stats1", 1, 2), (10, 1): ("apply2", 0, -1),
    (10, 2): ("apply2", 1, -1), (11, 0): ("apply2", 2, -1), (11, 1): ("apply2", 3, -1), (11, 2): ("stats1", 2, 2),
    (12, 2): ("mix_k", 0, -1), (13, 1): ("stats1", 3, 2), (13, 2): ("mix_k", 1, -1), (14, 2): ("mix_r", 0, -1),
    (14, 3): ("mix_r", 1, -1), (15, 0): ("aggr1", 0, 2),
}
EXTRAS_AHEAD = {(8, q): ("stats1", q, 2) for q in range(NT)} | {(9, 0): ("aggr1", 0, 2)}
WEIGHT_TASKS = {(4, 1): ("w", WR, 0), (8, 0): ("w", WF, 0), (12, 0): ("w", WO, 0)}
EARLY = {(11, 0): (9, 1)}
LATER = {(0, 0): (8, 0), (1, 0): (8, 1), (5, 0): (9, 0), (8, 0): (12, 1)}
PER_BATCH = {"oT": NG, "mT": NG, "xT": NC, "qk": 2 * NC, "v": NT // 2, "yT": NC, "fk": NC, "fr": NT // 2,
             "fv": NT // 2}


def build(nc, ids, e, wq, wk, wv, wr, wf, wo, mu, out):
    ctx = ExitStack()
    with ctx:
        def sb(name, shape, dt=F32):
            return ctx.enter_context(nc.sbuf_tensor(name, shape, dt))

        def pb(name, shape, dt=F32):
            return ctx.enter_context(nc.psum_tensor(name, shape, dt))

        def sem(name):
            return ctx.enter_context(nc.semaphore(name))

        q_stack = sb("q_stack", [P, H, T], BF16)
        k_stack = sb("k_stack", [P, H, T], BF16)
        probs = sb("probs", [P, 2 * GH, NT, T])
        v_aug = sb("v_aug", [P, NT, H, VW])
        v_new = sb("v_new", [P, NT, H, D])
        h_all = sb("h_all", [P, B * NT, C])
        xn = sb("xn", [P, NT, C])
        xnT = sb("xnT", [P, NC, T])
        qk_part = sb("qk_part", [P, 2 * NC, 3, T], BF16)
        rest = sb("rest", [P, 2, T])
        pvT = sb("pvT", [P, T])
        attn = sb("attn", [P, NT, C])
        h2 = sb("h2", [P, 2, NT, C])
        yn = sb("yn", [P, NT, C])
        ynT = sb("ynT", [P, NC, T + 1])
        dT = rest
        xrT = sb("xrT", [P, NC, T])
        xkT = sb("xkT", [P, NC, T])
        kaT = sb("kaT", [P, NC, T])
        tanh = sb("tanh", [P, NT, C])
        y = sb("y", [P, NT, C])
        wT = sb("wT", [P, 6, NC, C])
        w_nat = probs[:, 0:1, :, :].rearrange("p a b t -> p (a b t)")[:, 0:3 * NC * C].rearrange(
            "p (m r c) -> p m r c", m=3, r=NC)
        w_nat_mix = {WR: y[:, 0:NC, :], WF: y[:, NC:NT, :], WO: tanh[:, 0:NC, :]}
        ones = sb("ones", [NM, T], BF16)
        mu_c = sb("mu_c", [P, 2, NC])
        id_i = sb("id_i", [P, B * NT], I32)
        id_c = sb("id_c", [P, B * NT], I32)
        id_f = sb("id_f", [P, B * NT])
        id_g = sb("id_g", [P, B * NT])
        known = sb("known", [P, B * NT])
        ident = sb("ident", [P, P])
        ident_b = sb("ident_b", [P, P], BF16)
        stats = sb("stats", [P, 2, NT, 6])
        mean_var = sb("mean_var", [P, 2, NT, 2])
        rstd = sb("rstd", [P, 2, NT])
        half = sb("half", [P, NT])
        neg_max = sb("neg_max", [P, 2, GH, NT])
        m_rest = sb("m_rest", [P, 2, GH * NT])
        m_part = sb("m_part", [P, NM, GH * NT], BF16)
        mT = sb("mT", [NM * GH * NT, P], BF16)
        rden = sb("rden", [P, NT, GH])
        ps_st = [pb(f"ps_st{i}", [P, 2, T]) for i in range(2)]
        ps_mx = [pb(f"ps_mx{i}", [P, T]) for i in range(2)]
        ps_pv = pb("ps_pv", [P, T])
        ps_bg = pb("ps_bg", [P, T])

        w_loaded, ids_loaded, mu_loaded = sem("w_loaded"), sem("ids_loaded"), sem("mu_loaded")
        w_mix_loaded, ones_ready, ones_filled = sem("w_mix_loaded"), sem("ones_ready"), sem("ones_filled")
        gathered = [None, *(sem(f"gathered{i}") for i in range(1, B))]
        gathered_first = [sem(f"gathered_first{t}") for t in range(NT)]
        ids_ready, ident_zero, ident_ready = sem("ids_ready"), sem("ident_zero"), sem("ident_ready")
        id_step, consts_ready, masked = sem("id_step"), sem("consts_ready"), sem("masked")
        masked_ahead = sem("masked_ahead")
        w_psum, w_ready = sem("w_psum"), sem("w_ready")
        st_ready, exp_done = sem("st_ready"), sem("exp_done")
        mx_ready, mx_reduced = sem("mx_ready"), sem("mx_reduced")
        pv_done, pvT_ready = sem("pv_done"), sem("pvT_ready")
        filled = [sem(f"filled{c}") for c in range(NC)]
        filled_first = sem("filled_first")
        m_filled = [sem(f"m_filled{i}") for i in range(2)]
        m_step, m_split = sem("m_step"), sem("m_split")
        v_copied = sem("v_copied")
        part1_ready, rest_ready, part2_ready, rest2_ready, part3_ready = (
            sem("part1_ready"), sem("rest_ready"), sem("part2_ready"), sem("rest2_ready"), sem("part3_ready"))
        part_ready = (part1_ready, part2_ready, part3_ready)
        ln_stats = [sem("ln1_stats"), sem("ln2_stats")]
        ln_var = [sem("ln1_var"), sem("ln2_var")]
        ln_veps = [sem("ln1_veps"), sem("ln2_veps")]
        ln_rstd = [sem("ln1_rstd"), sem("ln2_rstd")]
        ln_done = [sem("ln1_done"), sem("ln2_done")]
        rden_ready, h2_ready, h2_first = sem("rden_ready"), sem("h2_ready"), sem("h2_first")
        d_ready, squared = sem("d_ready"), sem("squared")
        mixed = [sem("mixed_r"), sem("mixed_k")]
        y_ready, out_done = sem("y_ready"), sem("out_done")
        start_done = sem("start_done")
        full = {k: sem(f"{k}_full") for k in PER_BATCH}
        taken = {k: sem(f"{k}_taken") for k in PER_BATCH}

        def wait(eng, s, value):
            if not isinstance(value, int) or value > 0:
                eng.wait_ge(s, value)

        def fills(c, b):
            return 16 * (2 * NS * b - len(POOL_FILLS)) if c == 0 and b > 0 else 16 * 2 * NS * b

        def nth(kind, i, b):
            return PER_BATCH[kind] * b + (i + 1)

        def tasks_of(b):
            tasks = {at: (kind, i, b + who) for at, (kind, i, who) in TASKS.items() if 0 <= b + who < B}
            if b == 0:
                tasks |= WEIGHT_TASKS
            if b < 0:
                tasks = {EARLY.get(at, at): t for at, t in tasks.items()}
            if b >= B:
                tasks = {LATER.get(at, at): t for at, t in tasks.items()}
            return dict(sorted(tasks.items()))

        def extras_of(b):
            extras = {at: (kind, i, b + who) for at, (kind, i, who) in EXTRAS.items() if 0 <= b + who < B}
            if b < 0:
                extras = {at: x for at, x in extras.items() if x[0] != "stats1" and x[0] != "aggr1"}
                extras |= {at: (kind, i, b + who) for at, (kind, i, who) in EXTRAS_AHEAD.items()}
            return extras

        spare = [ps_bg, *(ps_st[i][:, k, :] for i in range(2) for k in range(2))]
        bank_of, occupant_before, latest = {}, {}, {m + 1: ("w", m, 0) for m in (WQ, WK, WV)}
        for b in range(-1, B + 2):
            for n, task in enumerate(tasks_of(b).values()):
                k = 0 if 0 <= b < B else n % len(spare)
                bank_of[task] = spare[k][:, :]
                occupant_before[task] = latest.get(k)
                latest[k] = task

        def sums_bank(gi):
            return ps_mx[0] if gi == NG * B - 1 else ps_pv

        block = ctx.enter_context(nc.Block())

        def mask(engine, n):
            return engine.tensor_scalar(h_all[:, n, :], h_all[:, n, :], known[:, n:n + 1], None, ALU.mult)

        def half_h2(engine, eng, i):
            b = B - 1
            wait(eng, y_ready, 2 * (b - 1))
            rows = slice(i * NT // 2, (i + 1) * NT // 2)
            return engine.tensor_tensor(h2[:, b % 2, rows, :], h_all[:, b * NT:(b + 1) * NT, :][:, rows, :],
                                        attn[:, rows, :], ALU.add)

        def token_difference(engine, c):
            return engine.tensor_tensor(dT[:, c, :], ynT[:, c, 1:T + 1], ynT[:, c, 0:T], ALU.subtract)

        def weight_out(copy, m, bank):
            for c in range(NC):
                src = bank[:, c * C:(c + 1) * C]
                dst = wT[:, m, c, :]
                if m in (WQ, WK):
                    src = src.rearrange("p (c h d) -> p c h d", c=NC, h=NH)
                    dst = dst.rearrange("p (c d h) -> p c h d", c=NC, h=NH)
                last = copy(dst, src)
            return last

        @block.sync
        def _(sp):
            nc.sync.dma_start(id_i[:], ids).then_inc(ids_loaded, 16)
            for m, w in ((WQ, wq), (WK, wk), (WV, wv)):
                nc.sync.dma_start(w_nat[:, m, :, :], w.rearrange("(r p) c -> p r c", p=P)).then_inc(w_loaded, 16)
            for m, w in ((WR, wr), (WF, wf), (WO, wo)):
                nc.sync.dma_start(w_nat_mix[m], w.rearrange("(r p) c -> p r c", p=P)
                                  ).then_inc(w_mix_loaded, 16)
            nc.sync.dma_start(mu_c[:], mu).then_inc(mu_loaded, 16)
            sp.wait_ge(ones_ready, 1)
            nc.sync.dma_start(k_stack[KS:KS + NM, :, :], ones[:, :].unsqueeze(1).broadcast_to([NM, H, T])
                              ).then_inc(ones_filled, 16)

            def fill(c, b):
                wait(sp, st_ready, 2 * H * (b - 1) + 2 * NH * (c + 1))
                for qk, part, s in FILLS:
                    if b == 0 and c == 0 and (qk, s) in POOL_FILLS:
                        continue
                    wait(sp, part_ready[part], 2 * NC * b + 2 * c + qk + 1)
                    nc.sync.dma_start((q_stack, k_stack)[qk][s * D:(s + 1) * D, c * NH:(c + 1) * NH, :],
                                      qk_part[:, 2 * c + qk, part, :]).then_inc(filled[c], 16)

            def fill_max(g, b):
                wait(sp, taken["mT"], nth("mT", g, b))
                wait(sp, st_ready, 2 * H * b + (8 * g + 8 - 2 * H))
                nc.sync.dma_start(q_stack[KS:KS + NM, g * GH:(g + 1) * GH, :], mT[:, :]).then_inc(m_filled[g % 2], 16)

            def iteration(b):
                nxt, cur, prv, prv2 = (0 <= b + who < B for who in (1, 0, -1, -2))
                for j in range(H):
                    if j == 0 and cur:
                        fill(1, b)
                    if j == 3 and cur:
                        fill_max(1, b)
                    if j == 7:
                        if cur:
                            fill_max(2, b)
                    if j == AT["fill0"] and nxt:
                        fill(0, b + 1)
                    if j == 11 and cur:
                        fill_max(3, b)
                    if j == (AT["out"] if cur else 15) and prv2:
                        for i in range(2):
                            wait(sp, y_ready, 2 * (b - 2) + i + 1)
                            rows = out[:, (b - 2) * NT + 2 * i:(b - 2) * NT + 2 * i + 2, :]
                            nc.sync.dma_start(rows, y[:, 2 * i:2 * i + 2, :]).then_inc(out_done, 16)
                    if j == 15 and nxt:
                        fill_max(0, b + 1)

            for b in range(-1, B + 2):
                iteration(b)
            sp.wait_ge(out_done, 2 * 16 * B)

        @block.gpsimd
        def _(pool):
            nc.gpsimd.memset(ident[:], 0.0).then_inc(ident_zero, 1)
            nc.gpsimd.memset(ident_b[:], 0.0).then_inc(ident_zero, 1)
            pool.wait_ge(ident_zero, 2)
            for m in (ident, ident_b):
                nc.gpsimd.affine_select(out=m[:], in_=m[:], compare_op=ALU.not_equal, fill=1.0, base=0,
                                        pattern=[[-1, P]], channel_multiplier=1).then_inc(ident_ready, 1)
            pool.wait_ge(ids_ready, 1)

            def gather(b):
                for t in range(b * NT, (b + 1) * NT):
                    nc.gpsimd.indirect_dma_start(h_all[:, t, :], None, e,
                                                 bass.IndirectOffsetOnAxis(ap=id_c[:, t:t + 1], axis=0)
                                                 ).then_inc(gathered[b] if b else gathered_first[t], 16)

            gather(0)
            nc.gpsimd.memset(half[:], -0.5).then_inc(consts_ready, 1)
            nc.gpsimd.memset(ynT[:, :, 0:1], 0.0).then_inc(consts_ready, 1)
            pool.wait_ge(consts_ready, 2)

            def rstd_of(ln, b):
                wait(pool, ln_stats[ln], b + 1)
                nc.gpsimd.tensor_scalar(rstd[:, ln, :], mean_var[:, ln, :, 1], EPS, None, ALU.add
                                        ).then_inc(ln_veps[ln], 1)
                wait(pool, ln_veps[ln], b + 1)
                nc.gpsimd.tensor_tensor(rstd[:, ln, :], rstd[:, ln, :], half[:], ALU.pow).then_inc(ln_rstd[ln], 1)

            def split_max(g, b):
                gi = NG * b + g
                wait(pool, mx_reduced, 16 * b + 16 * b * 3 + (16 * g + 16))
                nm = neg_max[:, g % 2, :, :].rearrange("p h t -> p (h t)")
                wait(pool, full["mT"], gi)
                nc.gpsimd.tensor_copy(m_part[:, 0, :], nm).then_inc(m_step, 1)
                wait(pool, m_step, 4 * gi + 1)
                nc.gpsimd.tensor_tensor(m_rest[:, 0, :], nm, m_part[:, 0, :], ALU.subtract).then_inc(m_step, 1)
                wait(pool, m_step, 4 * gi + 2)
                nc.gpsimd.tensor_copy(m_part[:, 1, :], m_rest[:, 0, :]).then_inc(m_step, 1)
                wait(pool, m_step, 4 * gi + 3)
                nc.gpsimd.tensor_tensor(m_rest[:, 1, :], m_rest[:, 0, :], m_part[:, 1, :], ALU.subtract).then_inc(m_step, 1)
                wait(pool, m_step, 4 * gi + 4)
                nc.gpsimd.tensor_copy(m_part[:, 2, :], m_rest[:, 1, :]).then_inc(m_split, 1)

            def third_part(i, b):
                wait(pool, part2_ready, 2 * NC * b + (i + 1))
                nc.gpsimd.tensor_tensor(qk_part[:, i, 2, :], rest[:, i % 2, :], qk_part[:, i, 1, :], ALU.subtract
                                        ).then_inc(part3_ready, 1)

            def iteration(b):
                nxt, cur, prv, prv2 = (0 <= b + who < B for who in (1, 0, -1, -2))
                for j in range(H):
                    if j == AT["mask"] and cur and b + 2 < B:
                        pool.wait_ge(gathered[b + 2], 16 * NT)
                        for t in range(NT):
                            mask(nc.gpsimd, (b + 2) * NT + t).then_inc(masked, 1)
                    if j == (AT["rstd1"] if cur else 9) and b + 2 < B:
                        rstd_of(0, b + 2)
                    if j == 1 and nxt and not cur:
                        rstd_of(0, b + 1)
                        if not cur:
                            nc.gpsimd.memset(v_aug[:], 1.0).then_inc(consts_ready, 1)
                            pool.wait_ge(consts_ready, 3)
                            gather(1)
                    if j == AT["gather"] and cur and b + 2 < B:
                        gather(b + 2)
                    if j in (2, 6, 10) and cur:
                        split_max((j + 2) // 4, b)
                    if j == 14 and nxt:
                        split_max(0, b + 1)
                    if 1 <= j <= NT and cur:
                        kt = j - 1
                        wait(pool, taken["v"], nth("v", kt // 2, b))
                        wait(pool, pv_done, 4 * NG * b + (kt - 3))
                        nc.gpsimd.tensor_copy(v_aug[:, kt, :, 0:D], v_new[:, kt, :, :]).then_inc(v_copied, 1)
                    for i in range(2 * NC):
                        if nxt and j == AT["third01" if i < 2 else "third23"]:
                            third_part(i, b + 1)
                        if b < 0 and j == AT["third01"] and i == 1:
                            pool.wait_ge(part2_ready, 2)
                            for _, s in POOL_FILLS:
                                nc.gpsimd.dma_start(k_stack[s * D:(s + 1) * D, 0:NH, :],
                                                    qk_part[:, 1, K_SLOTS[s], :]).then_inc(filled_first, 16)
                    if j == AT["h2"] and prv and cur:
                        wait(pool, taken["oT"], nth("oT", 3, b - 1))
                        wait(pool, y_ready, 2 * (b - 2))
                        nc.gpsimd.tensor_tensor(h2[:, (b - 1) % 2], h_all[:, (b - 1) * NT:b * NT, :], attn[:], ALU.add
                                                ).then_inc(h2_ready, 1)
                    if j == AT["h2"] and b == B:
                        wait(pool, taken["oT"], nth("oT", 3, B - 1))
                        half_h2(nc.gpsimd, pool, 1).then_inc(h2_ready, 1)
                    if j == AT["rstd2"] and prv:
                        rstd_of(1, b - 1)
                    if j == AT["d"] and prv and cur:
                        for c in range(NC):
                            wait(pool, taken["yT"], nth("yT", c, b - 1))
                            wait(pool, part3_ready, 2 * NC * min(b + 2, B))
                            wait(pool, mixed[0], NC * (b - 1))
                            wait(pool, mixed[1], NC * (b - 1))
                            token_difference(nc.gpsimd, c).then_inc(d_ready, 1)
                    if j == AT["squares"] and prv and cur:
                        for c in range(NC):
                            wait(pool, taken["fk"], nth("fk", c, b - 1))
                            nc.gpsimd.tensor_tensor(kaT[:, c, :], kaT[:, c, :], kaT[:, c, :], ALU.mult
                                                    ).then_inc(squared, 1)

            for b in range(-1, B + 2):
                iteration(b)

        @block.scalar
        def _(act):
            for m in (WQ, WK, WV):
                act.wait_ge(w_psum, m + 1)
                weight_out(nc.scalar.copy, m, spare[m + 1]).then_inc(w_ready, 1)

            def exponentials(b, j, p):
                n = 2 * (H * b + j) + p
                wait(act, st_ready, n + 1)
                if p == 0 and j % GH == 0:
                    wait(act, pv_done, 4 * NG * b + (j - 4))
                nc.scalar.activation(probs[:, j % (2 * GH), 2 * p:2 * p + 2, :], ps_st[p][:, :, :], ACT.Exp,
                                     scale=SCALE).then_inc(exp_done, 1)

            def second_part(i, b):
                wait(act, rest_ready, 2 * NC * b + (i + 1))
                nc.scalar.copy(qk_part[:, i, 1, :], rest[:, i % 2, :]).then_inc(part2_ready, 1)

            def background(task):
                kind, i, b = task
                if kind in ("oT", "fv"):
                    return
                if kind == "w":
                    act.wait_ge(w_psum, i + 1)
                    weight_out(nc.scalar.copy, i, ps_bg).then_inc(w_ready, 1)
                    return
                bank = bank_of[task]
                wait(act, full[kind], nth(kind, i, b))
                if kind == "xT":
                    wait(act, full["v"], 2 * b)
                    nc.scalar.copy(xnT[:, i, :], bank).then_inc(taken[kind], 1)
                if kind == "qk":
                    wait(act, filled[i // 2], fills(i // 2, b))
                    nc.scalar.copy(qk_part[:, i, 0, :], bank).then_inc(part1_ready, 1)
                if kind == "v":
                    wait(act, v_copied, NT * b)
                    nc.scalar.copy(v_new[:, 2 * i:2 * i + 2, :, :].rearrange("p t h d -> p (t h d)"), bank
                                   ).then_inc(taken[kind], 1)
                if kind == "mT":
                    g = NG * b + i
                    wait(act, m_filled[(i + 1) % 2], 16 * (2 * b + (i + 1) // 2))
                    nc.scalar.copy(mT[:], bank[0:NM * GH * NT, 0:P // 2].bitcast(BF16)).then_inc(taken[kind], 1)
                if kind == "yT":
                    wait(act, mixed[0], NC * b)
                    wait(act, mixed[1], NC * b)
                    nc.scalar.copy(ynT[:, i, 1:T + 1], bank).then_inc(taken[kind], 1)
                if kind == "fk":
                    wait(act, full["fv"], 2 * b)
                    nc.scalar.activation(kaT[:, i, :], bank, ACT.Relu).then_inc(taken[kind], 1)
                if kind == "fr":
                    wait(act, taken["fv"], 2 * b)
                    nc.scalar.activation(tanh[:, 2 * i:2 * i + 2, :].rearrange("p t c -> p (t c)"), bank,
                                         ACT.Tanh, scale=0.5).then_inc(taken[kind], 1)

            def iteration(b):
                nxt, cur, prv, prv2 = (0 <= b + who < B for who in (1, 0, -1, -2))
                tasks = tasks_of(b)
                for j in range(H):
                    done = j // GH - 2 if j % GH == 0 else None
                    if done is not None and (cur if done >= 0 else prv):
                        wait(act, pv_done, 4 * NG * b + (4 * done + 4))
                        wait(act, full["oT"], NG * b + done)
                        nc.scalar.copy(pvT[:], sums_bank(NG * b + done)[:]).then_inc(pvT_ready, 1)
                    for p in range(2):
                        if cur:
                            exponentials(b, j, p)
                        if (j, p) in tasks:
                            kind, i, whose = tasks[j, p]
                            background(tasks[j, p])
                            if kind == "qk" and not cur:
                                second_part(i, whose)
                        at = (j, 0) if p else (j - 1, 1)
                        if cur and at in tasks and tasks[at][0] == "qk":
                            second_part(*tasks[at][1:])

            for b in range(-1, B + 2):
                iteration(b)

        @block.vector
        def _(dve):
            vocab = e.shape[0]
            dve.wait_ge(ids_loaded, 16)
            nc.vector.tensor_copy(id_f[:], id_i[:]).then_inc(id_step, 1)
            dve.wait_ge(id_step, 1)
            nc.vector.tensor_scalar(id_g[:], id_f[:], 0.0, float(vocab - 1), ALU.max, ALU.min).then_inc(id_step, 1)
            dve.wait_ge(id_step, 2)
            nc.vector.tensor_copy(id_c[:], id_g[:]).then_inc(ids_ready, 1)
            nc.vector.tensor_tensor(known[:], id_f[:], id_g[:], ALU.is_equal).then_inc(id_step, 1)
            dve.wait_ge(id_step, 3)
            nc.vector.memset(ones[:], 1.0).then_inc(ones_ready, 1)


            def ln_statistics(ln, b, t):
                src = h_all[:, b * NT + t, :] if ln == 0 else h2[:, b % 2, t, :]
                nc.vector.bn_stats(stats[:, ln, t, :], src).then_inc(ln_var[ln], 1)

            def ln_aggregate(ln, b):
                wait(dve, ln_var[ln], NT * (b + 1))
                for t in range(NT):
                    last = nc.vector.bn_aggr(mean_var[:, ln, t, :], stats[:, ln, t, :])
                last.then_inc(ln_stats[ln], 1)

            def ln_apply(ln, b, tiles):
                wait(dve, ln_rstd[ln], b + 1)
                wait(dve, full["xT" if ln == 0 else "yT"], NC * b)
                for t in tiles:
                    src = h_all[:, b * NT + t, :] if ln == 0 else h2[:, b % 2, t, :]
                    nc.vector.tensor_scalar((xn, yn)[ln][:, t, :], src, mean_var[:, ln, t, 0:1],
                                            rstd[:, ln, t:t + 1], ALU.subtract, ALU.mult).then_inc(ln_done[ln], 1)

            def maxima(b, head, g, tiles):
                for t in tiles:
                    n = 4 * H * b + (4 * head + t)
                    wait(dve, mx_ready, n + 1)
                    if head % GH == 0 and t == 0:
                        wait(dve, m_split, NG * b + (g - 1))
                    nc.vector.tensor_reduce(neg_max[:, g % 2, head % GH, t:t + 1], ps_mx[t % 2][:], AX.X, ALU.max,
                                            negate=True).then_inc(mx_reduced, 1)

            def background(task, cur):
                kind, i, b = task
                bank = bank_of[task]
                if kind == "qk":
                    n = 2 * NC * b + i
                    wait(dve, part1_ready, n + 1)
                    wait(dve, part3_ready, n - 1)
                    nc.vector.tensor_tensor(rest[:, i % 2, :], bank, qk_part[:, i, 0, :], ALU.subtract
                                            ).then_inc(rest_ready, 1)
                if kind == "oT":
                    wait(dve, full["oT"], nth("oT", i, b))
                    sums = bank.rearrange("p (t h w) -> p t h w", t=NT, h=GH)
                    wait(dve, taken["oT"], NG * b + i)
                    nc.vector.reciprocal(rden[:], sums[:, :, :, D]).then_inc(rden_ready, 1)
                    wait(dve, rden_ready, NG * b + (i + 1))
                    if i == 0:
                        wait(dve, h2_ready, b)
                    dst = attn[:, :, i * GH * D:(i + 1) * GH * D].rearrange("p t (h d) -> p t h d", h=GH)
                    nc.vector.tensor_tensor(dst, sums[:, :, :, 0:D], rden[:, :, :].unsqueeze(3).broadcast_to([P, NT, GH, D]),
                                            ALU.mult).then_inc(taken["oT"], 1)
                if kind == "fv":
                    wait(dve, full["fv"], nth("fv", i, b))
                    wait(dve, taken["fr"], nth("fr", i, b))
                    wait(dve, out_done, 16 * 2 * b)
                    flat = lambda a: a[:, 2 * i:2 * i + 2, :].rearrange("p t c -> p (t c)")
                    nc.vector.scalar_tensor_tensor(flat(y), flat(tanh), 1.0, bank, ALU.add, ALU.mult
                                                   ).then_inc(taken["fv"], 1)
                    wait(dve, taken["fv"], nth("fv", i, b))
                    nc.vector.scalar_tensor_tensor(flat(y), flat(y), 0.5, flat(h2[:, b % 2]), ALU.mult, ALU.add
                                                   ).then_inc(y_ready, 1)
                if kind == "fk" and not cur:
                    wait(dve, taken["fk"], nth("fk", i, b))
                    nc.vector.tensor_tensor(kaT[:, i, :], kaT[:, i, :], kaT[:, i, :], ALU.mult).then_inc(squared, 1)

            def mix(m, dst, c, b):
                wait(dve, mu_loaded, 16)
                wait(dve, full["fk"] if m else full["fr"], 2 * b)
                wait(dve, d_ready, NC * b + (c + 1))
                nc.vector.scalar_tensor_tensor(dst[:, c, :], dT[:, c, :], mu_c[:, m, c:c + 1],
                                               ynT[:, c, 0:T], ALU.mult, ALU.add).then_inc(mixed[m], 1)

            def extra(kind, i, b):
                if kind == "stats1":
                    if b == 1:
                        dve.wait_ge(gathered[1], 16 * NT)
                        mask(nc.vector, NT + i).then_inc(masked_ahead, 1)
                        dve.wait_ge(masked_ahead, NT + i + 1)
                    else:
                        dve.wait_ge(masked, (b - 2) * NT + i + 1)
                    ln_statistics(0, b, i)
                if kind == "stats2":
                    if i == 0:
                        wait(dve, h2_ready, b + 1)
                    ln_statistics(1, b, i)
                if kind in ("aggr1", "aggr2"):
                    ln_aggregate(0 if kind == "aggr1" else 1, b)
                if kind in ("apply1", "apply2"):
                    ln_apply(0 if kind == "apply1" else 1, b, (i,))
                if kind == "mix_k":
                    mix(1, xkT, i, b)
                if kind == "mix_r":
                    mix(0, xrT, i, b)

            def iteration(b):
                nxt, cur, prv = (0 <= b + who < B for who in (1, 0, -1))
                tasks, extras = tasks_of(b), extras_of(b)
                for j in range(H):
                    head, ahead = (j + LEAD) % H, (j + LEAD) // H
                    if b < 0 and j == 0:
                        for t in range(NT):
                            dve.wait_ge(gathered_first[t], 16)
                            mask(nc.vector, t).then_inc(masked_ahead, 1)
                            dve.wait_ge(masked_ahead, t + 1)
                            ln_statistics(0, 0, t)
                        ln_aggregate(0, 0)
                    for q in range(NT):
                        if nxt if ahead else cur:
                            maxima(b + ahead, head, head // GH, (q,))
                        if q in (0, 2) and (j, q // 2) in tasks:
                            background(tasks[j, q // 2], cur)
                        if (j, q) in extras:
                            extra(*extras[j, q])

            def behind():
                b = B - 1
                tasks = {task[:2]: task for task in tasks_of(B).values()}
                background(tasks["oT", 2], False)
                background(tasks["oT", 3], False)
                wait(dve, taken["oT"], nth("oT", 3, b))
                half_h2(nc.vector, dve, 0).then_inc(h2_first, 1)
                wait(dve, h2_first, 1)
                for t in range(NT):
                    if t == NT // 2:
                        wait(dve, h2_ready, b + 1)
                    ln_statistics(1, b, t)
                ln_aggregate(1, b)
                ln_apply(1, b, range(NT))
                wait(dve, part3_ready, 2 * NC * B)
                for c in range(NC):
                    wait(dve, taken["yT"], nth("yT", c, b))
                    token_difference(nc.vector, c).then_inc(d_ready, 1)
                for m, dst in ((1, xkT), (0, xrT)):
                    for c in range(NC):
                        mix(m, dst, c, b)
                for kind in ("fv", "fk"):
                    for i in range(NC):
                        background(tasks[kind, i], False)

            for b in range(-1, B):
                iteration(b)
            behind()
            for task in tasks_of(B + 1).values():
                background(task, False)

        @block.tensor
        def _(pe):
            def keep_warm(n):
                for _ in range(n):
                    nc.tensor.transpose(ps_mx[1][:, 0:P], ident[:], ident[:])

            def transpose_weight(m, src, bank):
                for c in range(NC):
                    for r in range(NC):
                        last = nc.tensor.transpose(bank[:, c * C + r * P:c * C + (r + 1) * P],
                                                   src[:, r, c * P:(c + 1) * P], ident[:])
                last.then_inc(w_psum, 1)

            pe.wait_ge(ident_ready, 2)
            for m in (WQ, WK, WV):
                pe.wait_ge(w_loaded, 3 * 16)
                transpose_weight(m, w_nat[:, m], spare[m + 1])

            keep_warm(WARM[0])

            def scores_transposed(b, j, p):
                n = 2 * (H * b + j) + p
                if p == 0 and j % GH == 0:
                    g = j // GH
                    wait(pe, m_filled[g % 2], 16 * (2 * b + (g // 2 + 1)))
                wait(pe, exp_done, n - 1)
                for i in range(2):
                    kt = 2 * p + i
                    last = nc.tensor.matmul(ps_st[p][:, i, :], k_stack[0:KS + NM, j, kt * P:(kt + 1) * P],
                                            q_stack[0:KS + NM, j, :], start=True, stop=True)
                last.then_inc(st_ready, 1)

            def scores_for_max(b, head, tiles):
                if head % NH == 0 and tiles[0] == 0:
                    wait(pe, filled[head // NH], fills(head // NH, b + 1))
                    if b == 0 and head == 0:
                        wait(pe, filled_first, 16 * len(POOL_FILLS))
                for t in tiles:
                    n = 4 * H * b + (4 * head + t)
                    wait(pe, mx_reduced, n - 1)
                    nc.tensor.matmul(ps_mx[t % 2][:], q_stack[0:KS, head, t * P:(t + 1) * P], k_stack[0:KS, head, :],
                                     start=True, stop=True).then_inc(mx_ready, 1)

            def weighted_sums(b, g, kt):
                gi = NG * b + g
                if kt == 0:
                    wait(pe, exp_done, 8 * gi + 8)
                    if gi < NG * B - 1:
                        wait(pe, pvT_ready, gi)
                    else:
                        wait(pe, mx_reduced, H * NT * B)
                wait(pe, v_copied, NT * b + (kt + 1))
                for h in range(GH):
                    last = nc.tensor.matmul(sums_bank(gi)[h * VW:(h + 1) * VW, :], v_aug[:, kt, g * GH + h, :],
                                            probs[:, (g % 2) * GH + h, kt, :], start=(kt == 0), stop=(kt == NT - 1),
                                            tile_position=(0, h * VW))
                last.then_inc(pv_done, 1)

            def background(task):
                kind, i, b = task
                bank = bank_of[task]
                mm, last = nc.tensor.matmul, None
                if kind == "w":
                    wait(pe, w_mix_loaded, 3 * 16)
                    transpose_weight(i, w_nat_mix[i], bank)
                    return
                if kind in ("xT", "yT"):
                    ln = 0 if kind == "xT" else 1
                    wait(pe, ln_done[ln], NT * (b + 1))
                    for t in range(NT):
                        last = nc.tensor.transpose(bank[:, t * P:(t + 1) * P], (xn, yn)[ln][:, t, i * P:(i + 1) * P],
                                                   ident[:])
                if kind == "qk":
                    wait(pe, taken["xT"], NC * (b + 1))
                    wait(pe, w_ready, WV + 1)
                    tile, m = i // 2, (WQ, WK)[i % 2]
                    for c in range(NC):
                        last = mm(bank[:], wT[:, m, c, tile * P:(tile + 1) * P], xnT[:, c, :],
                                  start=(c == 0), stop=(c == NC - 1))
                if kind == "v":
                    for t in range(2):
                        for c in range(NC):
                            tok = 2 * i + t
                            last = mm(bank[:, t * C:(t + 1) * C], xnT[:, c, tok * P:(tok + 1) * P], wT[:, WV, c, :],
                                      start=(c == 0), stop=(c == NC - 1))
                if kind == "mT":
                    wait(pe, m_split, NG * b + (i + 1))
                    last = nc.tensor.transpose(bank[0:NM * GH * NT, 0:P // 2].bitcast(BF16),
                                               m_part[:, :, :].rearrange("p a n -> p (a n)"), ident_b[:])
                if kind == "oT":
                    wait(pe, pvT_ready, NG * b + (i + 1))
                    for t in range(NT):
                        last = nc.tensor.transpose(bank[:, t * P:(t + 1) * P], pvT[:, t * P:(t + 1) * P], ident[:])
                if kind == "fk":
                    wait(pe, mixed[1], NC * (b + 1))
                    wait(pe, w_ready, 6)
                    for c in range(NC):
                        last = mm(bank[:], wT[:, WF, c, i * P:(i + 1) * P], xkT[:, c, :],
                                  start=(c == 0), stop=(c == NC - 1))
                if kind == "fr":
                    wait(pe, mixed[0], NC * (b + 1))
                    for t in range(2):
                        for c in range(NC):
                            tok = 2 * i + t
                            last = mm(bank[:, t * C:(t + 1) * C], xrT[:, c, tok * P:(tok + 1) * P], wT[:, WR, c, :],
                                      start=(c == 0), stop=(c == NC - 1))
                if kind == "fv":
                    wait(pe, squared, NC * (b + 1))
                    for t in range(2):
                        for c in range(NC):
                            tok = 2 * i + t
                            last = mm(bank[:, t * C:(t + 1) * C], kaT[:, c, tok * P:(tok + 1) * P], wT[:, WO, c, :],
                                      start=(c == 0), stop=(c == NC - 1))
                last.then_inc(full[kind], 1)

            def out_of_bank(task):
                kind, i, b = task
                if kind == "w":
                    wait(pe, w_ready, i + 1)
                else:
                    wait(pe, rest_ready if kind == "qk" else taken[kind], nth(kind, i, b))

            def iteration(b):
                nxt, cur, prv, prv2 = (0 <= b + who < B for who in (1, 0, -1, -2))
                tasks = tasks_of(b)
                if b == 0:
                    for task in tasks_of(-1).values():
                        out_of_bank(task)
                    pe.wait_ge(ones_filled, 16)
                    pe.wait_ge(consts_ready, 3)

                for j in range(H):
                    head, ahead = (j + LEAD) % H, (j + LEAD) // H

                    def task_at(place):
                        task = tasks.get((j, place))
                        if b == -1 and (j, place) == (9, 1):
                            keep_warm(WARM[1])
                        if b == B and (j, place) == (10, 0):
                            keep_warm(WARM[2])
                        if b == B and (j, place) == (12, 1):
                            keep_warm(WARM[3])
                        if task is not None:
                            if occupant_before[task] is not None:
                                out_of_bank(occupant_before[task])
                            background(task)

                    def maximum(t):
                        if nxt if ahead else cur:
                            scores_for_max(b + ahead, head, (t,))

                    if cur:
                        scores_transposed(b, j, 0)
                    maximum(0)
                    task_at(0)
                    maximum(1)
                    if cur:
                        scores_transposed(b, j, 1)
                    maximum(2)
                    g = j // GH - 1
                    if cur if g >= 0 else prv:
                        weighted_sums(b + (0 if g >= 0 else -1), g % NG, j % GH)
                    task_at(1)
                    maximum(3)

            for b in range(-1, B + 2):
                iteration(b)


def kernel(x, L0_tok_e, L0_attn_Wq, L0_attn_Wk, L0_attn_Wv, L0_ffn_W_r, L0_ffn_W_k, L0_ffn_W_v, L0_ffn_mu_r,
           L0_ffn_mu_k):
    import numpy as np
    import concourse.bacc as bacc
    from concourse.bass_utils import run_bass_kernel_spmd

    nc = bacc.Bacc("TRN2", target_bir_lowering=False, num_devices=1)
    arrays = {
        "ids": np.ascontiguousarray(np.asarray(x).reshape(B * NT, P).T),
        "e": np.asarray(L0_tok_e),
        "wq": np.asarray(L0_attn_Wq), "wk": np.asarray(L0_attn_Wk), "wv": np.asarray(L0_attn_Wv),
        "wr": np.asarray(L0_ffn_W_r), "wf": np.asarray(L0_ffn_W_k), "wo": np.asarray(L0_ffn_W_v),
        "mu": np.ascontiguousarray(np.stack([np.asarray(L0_ffn_mu_r), np.asarray(L0_ffn_mu_k)])
                                   .reshape(2, NC, P).transpose(2, 0, 1)),
    }
    args = [nc.dram_tensor(n, a.shape, mybir.dt.from_np(a.dtype), kind="ExternalInput").ap()
            for n, a in arrays.items()]
    out = nc.dram_tensor("out", (B * NT * P, C), F32, kind="ExternalOutput").ap()
    build(nc, *args, out.rearrange("(n p) c -> p n c", p=P))
    r = run_bass_kernel_spmd(nc, [arrays], core_ids=[0])
    return np.asarray(r.results[0]["out"]).reshape(B, T, C)
```
